# Optimizing a Trainium2 kernel written in Bass

```python
import numpy as np
import jax
import jax.numpy as jnp

def _softmax(x, axis=-1):
    return jax.nn.softmax(x, axis=axis)

def _gelu(x):
    return jax.nn.gelu(x, approximate=True)

def _silu(x):
    return jax.nn.silu(x)

def _sigmoid(x):
    return jax.nn.sigmoid(x)

def _layernorm(x, axis=-1, eps=1e-05):
    m = jnp.mean(x, axis=axis, keepdims=True)
    v = jnp.var(x, axis=axis, keepdims=True)
    return (x - m) / jnp.sqrt(v + eps)

def _scatter_add(tgt, idx, src, axis=0):
    return tgt.at[idx].add(src)

def _segment_sum(src, seg, n):
    return jax.ops.segment_sum(src, seg, n)
kernel_name = 'mk_adj_preln_d2_adj_r2_05ae72'

def setup_inputs(seed: int=0):
    np.random.seed(seed)
    _w = jnp.asarray

    def _rec_inputs():
        import jax
        import jax.numpy as jnp
        _gk = jax.random.key(seed)
        x = -0.0005207 + 1.001 * jax.random.normal(jax.random.fold_in(_gk, 1), (4096, 128), jnp.float32)
        _a = jax.random.bernoulli(jax.random.fold_in(_gk, 2), 0.00195312, (4096, 4096))
        _a = jnp.logical_or(_a, jnp.swapaxes(_a, -1, -2))
        _a = jnp.logical_or(_a, jnp.eye(4096, dtype=bool))
        _af = _a.astype(jnp.float32)
        _af = _af * jax.random.uniform(jax.random.fold_in(_gk, 3), (4096, 4096), jnp.float32, 0.05, 1)
        adj = _af
        return (x, adj)
    x, adj = _rec_inputs()

    def _L0_gnn_setup():
        import jax, jax.numpy as jnp
        import numpy as np
        N = 4096
        F_IN = 128
        F_OUT = 128
        key = jax.random.key(seed)
        k1, k2, k3, k4 = jax.random.split(key, 4)
        return {'input': jax.random.normal(k1, (N, F_IN), dtype=jnp.float32), 'adj': jax.random.uniform(k2, (N, N), dtype=jnp.float32), 'weight': jax.random.normal(k3, (F_IN, F_OUT), dtype=jnp.float32) * (1.0 / np.sqrt(F_OUT)), 'bias': jax.random.normal(k4, (F_OUT,), dtype=jnp.float32) * (1.0 / np.sqrt(F_OUT))}
    _L0_gnn_all = _L0_gnn_setup()
    _L0_gnn_in = {k: v for k, v in _L0_gnn_all.items() if k in ('weight', 'bias')}
    del _L0_gnn_all

    def _L1_gnn_setup():
        import jax, jax.numpy as jnp
        import numpy as np
        N = 4096
        D = 128
        CUTOFF = 1.0
        MU = 1.0
        SIGMA = 0.5

        def sensitivity(r, mu, sigma):
            return jnp.exp(-(1.0 / r - 1.0 / mu) ** 2 / (2.0 * sigma * sigma))
        key = jax.random.key(seed)
        k_z, k_d, k_w = jax.random.split(key, 3)
        z = jax.random.normal(k_z, (N, D), dtype=jnp.float32)
        dist_matrix = jax.random.uniform(k_d, (N, N), dtype=jnp.float32) * 2.0 + 0.05
        W = jax.random.normal(k_w, (D, D), dtype=jnp.float32)
        B = jnp.zeros((D,), dtype=jnp.float32)
        return {'z': z, 'dist_matrix': dist_matrix, 'W': W, 'B': B}
    _L1_gnn_all = _L1_gnn_setup()
    _L1_gnn_in = {k: v for k, v in _L1_gnn_all.items() if k in ('W', 'B')}
    del _L1_gnn_all
    return {'x': x, 'adj': adj, 'L0_gnn_weight': _L0_gnn_in['weight'], 'L0_gnn_bias': _L0_gnn_in['bias'], 'L1_gnn_W': _L1_gnn_in['W'], 'L1_gnn_B': _L1_gnn_in['B']}

def reference(x, adj, L0_gnn_weight, L0_gnn_bias, L1_gnn_W, L1_gnn_B):
    import jax
    import jax.numpy as jnp

    def _L0_gnn_ref(input, adj, weight, bias):
        import jax, jax.numpy as jnp
        import numpy as np
        N = 4096
        F_IN = 128
        F_OUT = 128
        n = input.shape[0]
        a = adj + jnp.eye(n, dtype=adj.dtype)
        d = jax.lax.rsqrt(jnp.sum(a, axis=1))
        adj_norm = d[:, None] * a * d[None, :]
        support = input @ weight
        out = adj_norm @ support + bias
        return out

    def _L1_gnn_ref(z, dist_matrix, W, B):
        import jax, jax.numpy as jnp
        import numpy as np
        N = 4096
        D = 128
        CUTOFF = 1.0
        MU = 1.0
        SIGMA = 0.5

        def sensitivity(r, mu, sigma):
            return jnp.exp(-(1.0 / r - 1.0 / mu) ** 2 / (2.0 * sigma * sigma))
        msg = z @ W + B
        sens = sensitivity(dist_matrix, MU, SIGMA)
        weights = jnp.where(dist_matrix < CUTOFF, sens, 0.0)
        return weights @ msg
    h = jnp.maximum(_layernorm(x, axis=-1), 0.0)
    x = x + _L0_gnn_ref(h, adj, L0_gnn_weight, L0_gnn_bias)
    h = jnp.maximum(_layernorm(x, axis=-1), 0.0)
    x = x + _L1_gnn_ref(h, adj, L1_gnn_W, L1_gnn_B)
    return x

_drawn_inputs = setup_inputs


def setup_inputs(seed=0):
    import zlib

    import numpy as np

    out = dict(_drawn_inputs(seed))
    spreads = {'L1_gnn_B': (0.0, 0.388)}
    factors = {}
    for name, (base, spread) in spreads.items():
        noise = np.random.default_rng([zlib.crc32(name.encode()), seed]).standard_normal(out[name].shape)
        drawn = base * np.exp(spread * noise) if base else spread * noise
        out[name] = jnp.asarray(drawn.astype(out[name].dtype))
    for name, factor in factors.items():
        out[name] = (out[name] * factor).astype(out[name].dtype)
    return out
```

```python
import concourse.bass as bass
from concourse import mybir
from contextlib import ExitStack

P = 128
N = 4096
D = 128
SUB = 4
SLAB = SUB * P
SLABS = N // SLAB
CHUNK = 1024
CHUNKS = N // CHUNK
KB = N // P
KC = KB // CHUNKS
PIECES = 2
PIECE = SUB * CHUNK // PIECES
TEMPS = 4
TBANKS = 4
EVACS = 4
EPS = 1e-5
TINY, HUGE = 2.0 ** -60, 2.0 ** 60
SIGN = -2 ** 31


def graph_layers(nc, x, adj, w0, b0, w1, b1, out):
    f32, i32 = mybir.dt.float32, mybir.dt.int32
    ALU, ACT, AX = mybir.AluOpType, mybir.ActivationFunctionType, mybir.AxisListType

    adj_v = adj.rearrange("(g s p) (c n) -> g c p s n", p=P, s=SUB, n=CHUNK)
    x_v = x.rearrange("(t p) f -> p t f", p=P)
    out_v = out.rearrange("(g s p) f -> g p s f", p=P, s=SUB)

    ctx = ExitStack()
    with ctx:
        def sb(name, shape, dt=f32):
            return ctx.enter_context(nc.sbuf_tensor(name, shape, dt))

        def pb(name, shape):
            return ctx.enter_context(nc.psum_tensor(name, shape, f32))

        def sem(name):
            return ctx.enter_context(nc.semaphore(name))

        chunk = [sb(f"chunk{c}", [P, SUB, CHUNK]) for c in range(CHUNKS)]
        temp = [sb(f"temp{n}", [P, PIECE]) for n in range(TEMPS)]
        block_t = [sb(f"block_t{n}", [P, SLAB]) for n in range(EVACS)]
        tokens = sb("tokens", [P, KB, D])
        support = sb("support", [P, KB, D])
        message = sb("message", [P, KB, D])
        weight = [sb("weight0", [P, D]), sb("weight1", [P, D])]
        bias = [sb("bias0", [P, D]), sb("bias1", [P, D])]
        ident = sb("ident", [P, P])
        row_part = sb("row_part", [P, KB, CHUNKS])
        degree = sb("degree", [P, KB])
        dinv = sb("dinv", [P, KB])
        dtmp = sb("dtmp", [P, KB])
        mean = sb("mean", [P, SUB])
        var = sb("var", [P, SUB])
        rstd = sb("rstd", [P, SUB])
        rtmp = sb("rtmp", [P, SUB])
        rtmp_act = sb("rtmp_act", [P, SUB])
        dtmp_act = sb("dtmp_act", [P, KB])
        centred = sb("centred", [P, SUB, D])
        squares = sb("squares", [P, SUB, D])
        hidden = sb("hidden", [P, SUB, D])
        hidden_t = sb("hidden_t", [P, SLAB])
        acc_t = sb("acc_t", [P, SLAB])
        mixed = sb("mixed", [P, SUB, D])
        result = sb("result", [P, SUB, D])

        tbank = [pb(f"tbank{n}", [P, SLAB]) for n in range(TBANKS)]
        acc = pb("acc", [P, SLAB])
        hbank = pb("hbank", [P, SLAB])
        xbank = pb("xbank", [P, SUB, D])

        inputs_in = sem("inputs_in")
        loaded = [sem(f"loaded{c}") for c in range(CHUNKS)]
        ident_made = sem("ident_made")
        summed = sem("summed")
        dve_step = sem("dve_step")
        var_ready = sem("var_ready")
        rstd_seed = sem("rstd_seed")
        act_step = sem("act_step")
        ln_done = sem("ln_done")
        square_done = sem("square_done")
        hidden_ready = sem("hidden_ready")
        hidden_turned = sem("hidden_turned")
        hidden_t_ready = sem("hidden_t_ready")
        projected = sem("projected")
        support_raw = sem("support_raw")
        degree_ready = sem("degree_ready")
        dinv_seed = sem("dinv_seed")
        support_ready = sem("support_ready")
        bias_added = sem("bias_added")
        turned = sem("turned")
        evacuated = sem("evacuated")
        multiplied = sem("multiplied")
        acc_out = sem("acc_out")
        acc_turned = sem("acc_turned")
        message_ready = sem("message_ready")
        squared = sem("squared")
        clamped = sem("clamped")
        inverted = sem("inverted")
        signed = sem("signed")
        expd = sem("expd")
        weighed = sem("weighed")
        result_ready = sem("result_ready")
        stored = sem("stored")

        block = ctx.enter_context(nc.Block())

        def wait(eng, s, value):
            if not isinstance(value, int) or value > 0:
                eng.wait_ge(s, value)

        def of_slab(t, g):
            return t[:, bass.ds(g * SUB, SUB)]

        def per_row(t):
            return t.unsqueeze(2).to_broadcast([P, SUB, D])

        @block.sync
        def _(sp):
            sp.dma_start(tokens[:, :, :], x_v).then_inc(inputs_in, 16)
            sp.dma_start(weight[0][:, :], w0).then_inc(inputs_in, 16)
            sp.dma_start(weight[1][:, :], w1).then_inc(inputs_in, 16)
            for n, b in enumerate((b0, b1)):
                sp.dma_start(bias[n][:, :], b.rearrange("(o f) -> o f", o=1).to_broadcast([P, D])).then_inc(inputs_in, 16)

            def load(g, c):
                sp.dma_start(chunk[c][:, :, :], adj_at(g, c)).then_inc(loaded[c], 16)

            def adj_at(g, c):
                if isinstance(g, int):
                    return adj_v[g, c]
                return adj_v[bass.ds(g, 1), c].squeeze(0)

            for c in range(CHUNKS):
                load(0, c)
            with sp.Fori(1, SLABS) as g:
                for c in range(CHUNKS):
                    sp.wait_ge(summed, CHUNKS * (g - 1) + c + 1)
                    load(g, c)
            for turn in range(2):
                for c in range(CHUNKS):
                    if turn == 0:
                        sp.wait_ge(summed, CHUNKS * (SLABS - 1) + c + 1)
                    else:
                        sp.wait_ge(turned, KB * (SLABS - 1) + KC * (c + 1))
                    load(0, c)
                with sp.Fori(1, SLABS) as g:
                    for c in range(CHUNKS):
                        sp.wait_ge(turned, KB * (turn * SLABS + g - 1) + KC * (c + 1))
                        load(g, c)

        @block.gpsimd
        def _(pool):
            pool.memset(ident[:, :], 0.0).then_inc(ident_made, 1)
            pool.wait_ge(ident_made, 1)
            pool.affine_select(out=ident[:, :], in_=ident[:, :], compare_op=ALU.not_equal, fill=1.0, base=0,
                               pattern=[[-1, P]], channel_multiplier=1).then_inc(ident_made, 1)
            pool.wait_ge(inputs_in, 5 * 16)
            pool.wait_ge(hidden_ready, SLABS)
            pool.tensor_tensor(tokens[:, :, :], tokens[:, :, :],
                               bias[0][:, :].unsqueeze(1).to_broadcast([P, KB, D]), ALU.add).then_inc(bias_added, 1)

            def store(g):
                pool.wait_ge(result_ready, g + 1)
                dst = out_v[g] if isinstance(g, int) else out_v[bass.ds(g, 1)].squeeze(0)
                pool.dma_start(dst, result[:, :, :]).then_inc(stored, 16)

            def square(g, c, h):
                m = PIECES * (CHUNKS * g + c) + h
                t = temp[(PIECES * c + h) % TEMPS]
                rows = SUB // PIECES
                a = chunk[c][:, h * rows:(h + 1) * rows, :].rearrange("p s n -> p (s n)")
                if h == 0:
                    pool.wait_ge(loaded[c], 16 * (2 * SLABS + g + 1))
                wait(pool, weighed, m - TEMPS + 1)
                pool.tensor_tensor(t[:, :], a, a, ALU.mult).then_inc(squared, 1)

            def slab(g):
                for c in range(CHUNKS):
                    for h in range(PIECES):
                        square(g, c, h)

            slab(0)
            with pool.Fori(1, SLABS) as g:
                slab(g)
                store(g - 1)
            store(SLABS - 1)
            pool.wait_ge(stored, 16 * SLABS)

        @block.tensor
        def _(pe):
            def turn_hidden(n):
                pe.wait_ge(hidden_ready, n + 1)
                wait(pe, hidden_t_ready, n)
                for s in range(SUB):
                    last = pe.transpose(hbank[:, bass.ts(s, P)], hidden[:, s, :], ident[:, :])
                last.then_inc(hidden_turned, 1)

            def project(n, w):
                pe.wait_ge(hidden_t_ready, n + 1)
                for s in range(SUB):
                    last = pe.matmul(xbank[:, s, :], hidden_t[:, bass.ts(s, P)], weight[w][:, :], start=True, stop=True)
                last.then_inc(projected, 1)

            def turn_acc(n):
                pe.wait_ge(acc_out, n + 1)
                for s in range(SUB):
                    last = pe.transpose(xbank[:, s, :], acc_t[:, bass.ts(s, P)], ident[:, :])
                last.then_inc(acc_turned, 1)

            def turn_block(turn, g, k):
                n = KB * (turn * SLABS + g) + k
                c, kc = divmod(k, KC)
                if kc == 0:
                    if turn == 0:
                        pe.wait_ge(loaded[c], 16 * (SLABS + g + 1))
                    else:
                        pe.wait_ge(weighed, PIECES * (CHUNKS * g + c + 1))
                wait(pe, evacuated, n - TBANKS + 1)
                for s in range(SUB):
                    last = pe.transpose(tbank[k % TBANKS][:, bass.ts(s, P)], chunk[c][:, s, bass.ts(kc, P)], ident[:, :])
                last.then_inc(turned, 1)

            def multiply(turn, g, k):
                n = KB * (turn * SLABS + g) + k
                if k == 0:
                    wait(pe, acc_out, turn * SLABS + g)
                if k % SUB == 0:
                    if turn == 0:
                        pe.wait_ge(support_ready, k // SUB + 1)
                    else:
                        pe.wait_ge(message_ready, k // SUB + 1)
                pe.wait_ge(evacuated, n + 1)
                stationary = (support, message)[turn]
                pe.matmul(acc[:, :], stationary[:, k, :], block_t[k % EVACS][:, :], start=k == 0,
                          stop=k == KB - 1).then_inc(multiplied, 1)

            def slab(turn, g, before):
                ahead = TBANKS - 1
                n = turn * SLABS + g
                for k in range(ahead):
                    turn_block(turn, g, k)
                for k in range(KB):
                    if k + ahead < KB:
                        turn_block(turn, g, k + ahead)
                    multiply(turn, g, k)
                    if before and k == 2:
                        if before == "message":
                            pe.wait_ge(support_raw, SLABS)
                            wait(pe, message_ready, n - 1)
                        else:
                            pe.wait_ge(message_ready, SLABS)
                            wait(pe, result_ready, n - SLABS - 1)
                        turn_acc(n - 1)
                    if before == "message" and k == 14:
                        turn_hidden(SLABS + n - 1)
                    if before == "message" and k == 18:
                        project(SLABS + n - 1, 1)

            pe.wait_ge(ident_made, 2)
            pe.wait_ge(inputs_in, 5 * 16)
            turn_hidden(0)
            project(0, 0)
            with pe.Fori(1, SLABS) as g:
                turn_hidden(g)
                pe.wait_ge(support_raw, g)
                project(g, 0)
            slab(0, 0, None)
            with pe.Fori(1, SLABS) as g:
                slab(0, g, "message")
            slab(1, 0, "message")
            with pe.Fori(1, SLABS) as g:
                slab(1, g, "result")
            pe.wait_ge(result_ready, SLABS - 1)
            turn_acc(2 * SLABS - 1)

        @block.scalar
        def _(act):
            def seed(done, source, result_, tmp, bias_, ready, step):
                done()
                act.activation(tmp, source, ACT.Ln, bias=bias_).then_inc(act_step, 1)
                act.wait_ge(act_step, step)
                act.activation(result_, tmp, ACT.Exp, scale=-0.5).then_inc(ready, 1)

            def norm_seed(n):
                seed(lambda: act.wait_ge(var_ready, n + 1), var[:, :], rstd[:, :], rtmp_act[:, :], 0.0, rstd_seed, n + 1)

            def relu_hidden(n):
                act.wait_ge(hidden_turned, n + 1)
                wait(act, projected, n)
                act.activation(hidden_t[:, :], hbank[:, :], ACT.Relu).then_inc(hidden_t_ready, 1)

            def copy_acc(n):
                act.wait_ge(multiplied, KB * (n + 1))
                wait(act, acc_turned, n)
                act.activation(acc_t[:, :], acc[:, :], ACT.Copy).then_inc(acc_out, 1)

            def copy_support(g):
                act.wait_ge(projected, g + 1)
                act.activation(of_slab(support, g), xbank[:, :, :], ACT.Copy).then_inc(support_raw, 1)

            def invert(m):
                t = temp[m_static(m)]
                act.wait_ge(clamped, m[0] + 1)
                act.activation(t[:, :], t[:, :], ACT.Ln).then_inc(ln_done, 1)
                act.wait_ge(ln_done, m[0] + 1)
                act.activation(t[:, :], t[:, :], ACT.Exp, scale=-0.5).then_inc(inverted, 1)

            def gaussian(m):
                t = temp[m_static(m)]
                act.wait_ge(signed, m[0] + 1)
                act.activation(t[:, :], t[:, :], ACT.Square, bias=1.0, scale=-1.0).then_inc(square_done, 1)
                act.wait_ge(square_done, m[0] + 1)
                act.activation(t[:, :], t[:, :], ACT.Exp, scale=-2.0).then_inc(expd, 1)

            def m_static(m):
                return m[1]

            act.preload_act_table_set("natural_log_exp_and_others")
            norm_seed(0)
            relu_hidden(0)
            copy_support(0)
            with act.Fori(1, SLABS) as g:
                norm_seed(g)
                relu_hidden(g)
                copy_support(g)
            seed(lambda: act.wait_ge(degree_ready, 1), degree[:, :], dinv[:, :], dtmp_act[:, :], 0.0, dinv_seed, SLABS + 1)
            def finish_message(n):
                copy_acc(n)
                seed(lambda: act.wait_ge(var_ready, SLABS + n + 1), var[:, :], rstd[:, :], rtmp_act[:, :], 0.0,
                     rstd_seed, SLABS + n + 2)
                relu_hidden(SLABS + n)

            with act.Fori(0, SLABS - 1) as g:
                finish_message(g)

            def piece(g, c, h):
                return PIECES * (CHUNKS * g + c) + h, (PIECES * c + h) % TEMPS

            for h in range(PIECES):
                invert(piece(0, 0, h))

            def weigh_step(g, c, more):
                for h in range(PIECES):
                    gaussian(piece(g, c, h))
                if more:
                    for h in range(PIECES):
                        invert(piece(g if c + 1 < CHUNKS else g + 1, (c + 1) % CHUNKS, h))

            weigh_step(0, 0, True)
            copy_acc(SLABS - 1)
            weigh_step(0, 1, True)
            seed(lambda: act.wait_ge(var_ready, 2 * SLABS), var[:, :], rstd[:, :], rtmp_act[:, :], 0.0,
                 rstd_seed, 2 * SLABS + 1)
            weigh_step(0, 2, True)
            relu_hidden(2 * SLABS - 1)
            weigh_step(0, 3, True)
            with act.Fori(1, SLABS - 1) as g:
                weigh_step(g, 0, True)
                copy_acc(SLABS + g - 1)
                for c in range(1, CHUNKS):
                    weigh_step(g, c, True)
            g = SLABS - 1
            weigh_step(g, 0, True)
            copy_acc(SLABS + g - 1)
            for c in range(1, CHUNKS):
                weigh_step(g, c, c + 1 < CHUNKS)
            copy_acc(2 * SLABS - 1)

        @block.vector
        def _(dve):
            NORM_STEPS = 9
            MIX_STEPS = 3
            DEGREE_STEPS = 5

            def link(base, j, ins):
                ins.then_inc(dve_step, 1)
                dve.wait_ge(dve_step, base + j)

            def norm_mean(base):
                link(base, 1, dve.reduce_sum(mean[:, :], norm_in[0], axis=AX.X))
                link(base, 2, dve.tensor_scalar(mean[:, :], mean[:, :], 1.0 / D, None, ALU.mult))

            def norm_centre(base):
                link(base, 3, dve.tensor_tensor(centred[:, :, :], norm_in[0], per_row(mean[:, :]), ALU.subtract))

            def norm_squares(base):
                link(base, 4, dve.tensor_tensor(squares[:, :, :], centred[:, :, :], centred[:, :, :], ALU.mult))

            def norm_var(base):
                link(base, 5, dve.reduce_sum(var[:, :], squares[:, :, :], axis=AX.X))
                dve.tensor_scalar(var[:, :], var[:, :], 1.0 / D, EPS, ALU.mult, ALU.add).then_inc(var_ready, 1)

            def norm_out(base, n):
                dve.wait_ge(rstd_seed, n + 1)
                link(base, 6, dve.tensor_tensor(rtmp[:, :], rstd[:, :], rstd[:, :], ALU.mult))
                link(base, 7, dve.tensor_tensor(rtmp[:, :], rtmp[:, :], var[:, :], ALU.mult))
                link(base, 8, dve.tensor_scalar(rtmp[:, :], rtmp[:, :], -0.5, 1.5, ALU.mult, ALU.add))
                link(base, 9, dve.tensor_tensor(rstd[:, :], rstd[:, :], rtmp[:, :], ALU.mult))
                wait(dve, hidden_turned, n)
                dve.tensor_tensor(hidden[:, :, :], centred[:, :, :], per_row(rstd[:, :]), ALU.mult)\
                   .then_inc(hidden_ready, 1)

            norm_in = [None]

            def row_sums(g, c):
                dve.wait_ge(loaded[c], 16 * (g + 1))
                dve.reduce_sum(row_part[:, bass.ds(g * SUB, SUB), c], chunk[c][:, :, :], axis=AX.X).then_inc(summed, 1)

            def norm(n, g):
                base = NORM_STEPS * n
                norm_in[0] = of_slab(tokens, g)
                norm_mean(base)
                norm_centre(base)
                norm_squares(base)
                norm_var(base)
                return base

            dve.wait_ge(inputs_in, 5 * 16)

            def pass1(g):
                base = norm(g, g)
                row_sums(g, 0)
                row_sums(g, 1)
                norm_out(base, g)
                row_sums(g, 2)
                row_sums(g, 3)

            pass1(0)
            with dve.Fori(1, SLABS) as g:
                pass1(g)
            base = NORM_STEPS * SLABS
            dve.wait_ge(summed, CHUNKS * SLABS)
            link(base, 1, dve.reduce_sum(degree[:, :], row_part[:, :, :], axis=AX.X))
            dve.tensor_scalar(degree[:, :], degree[:, :], 1.0, None, ALU.add).then_inc(degree_ready, 1)
            dve.wait_ge(dinv_seed, 1)
            link(base, 2, dve.tensor_tensor(dtmp[:, :], dinv[:, :], dinv[:, :], ALU.mult))
            link(base, 3, dve.tensor_tensor(dtmp[:, :], dtmp[:, :], degree[:, :], ALU.mult))
            link(base, 4, dve.tensor_scalar(dtmp[:, :], dtmp[:, :], -0.5, 1.5, ALU.mult, ALU.add))
            link(base, 5, dve.tensor_tensor(dinv[:, :], dinv[:, :], dtmp[:, :], ALU.mult))
            dve.wait_ge(support_raw, SLABS)
            for g in range(SLABS):
                dve.tensor_tensor(of_slab(support, g), of_slab(support, g), per_row(of_slab(dinv, g)), ALU.mult)\
                   .then_inc(support_ready, 1)
            base += DEGREE_STEPS
            PASS2 = base
            dve.wait_ge(support_ready, SLABS)
            dve.wait_ge(bias_added, 1)

            def evacuate(turn, g, k):
                n = KB * (turn * SLABS + g) + k
                dve.wait_ge(turned, n + 1)
                wait(dve, multiplied, n - EVACS + 1)
                dve.tensor_copy(block_t[k % EVACS][:, :], tbank[k % TBANKS][:, :]).then_inc(evacuated, 1)

            def finish_message(n, k):
                base = PASS2 + (MIX_STEPS + NORM_STEPS) * n
                x1 = of_slab(tokens, n)
                if k == 4:
                    dve.wait_ge(acc_turned, n + 1)
                    link(base, 1, dve.tensor_tensor(mixed[:, :, :], xbank[:, :, :], of_slab(support, n), ALU.add))
                if k == 5:
                    link(base, 2, dve.tensor_tensor(mixed[:, :, :], mixed[:, :, :], per_row(of_slab(dinv, n)), ALU.mult))
                if k == 6:
                    link(base, 3, dve.tensor_tensor(x1, x1, mixed[:, :, :], ALU.add))
                base = base + MIX_STEPS
                norm_in[0] = x1
                if k == 7:
                    norm_mean(base)
                if k == 8:
                    norm_centre(base)
                if k == 9:
                    norm_squares(base)
                if k == 10:
                    norm_var(base)
                if k == 12:
                    norm_out(base, SLABS + n)
                if k == 20:
                    dve.wait_ge(projected, SLABS + n + 1)
                    dve.tensor_tensor(of_slab(message, n), xbank[:, :, :],
                                      bias[1][:, :].unsqueeze(1).to_broadcast([P, SUB, D]), ALU.add)\
                       .then_inc(message_ready, 1)

            for k in range(KB):
                evacuate(0, 0, k)
            with dve.Fori(1, SLABS) as g:
                for k in range(KB):
                    evacuate(0, g, k)
                    finish_message(g - 1, k)

            def piece(g, c, h):
                rows = SUB // PIECES
                a = chunk[c][:, h * rows:(h + 1) * rows, :].rearrange("p s n -> p (s n)")
                return PIECES * (CHUNKS * g + c) + h, temp[(PIECES * c + h) % TEMPS], a

            def clamp(g, c, h):
                m, t, a = piece(g, c, h)
                dve.wait_ge(squared, m + 1)
                dve.tensor_scalar(t[:, :], t[:, :], HUGE, TINY, ALU.min, ALU.max).then_inc(clamped, 1)

            def sign(g, c, h):
                m, t, a = piece(g, c, h)
                dve.wait_ge(inverted, m + 1)
                ti = t[:, :].bitcast(i32)
                dve.scalar_tensor_tensor(ti, a.bitcast(i32), SIGN, ti, ALU.bitwise_and, ALU.bitwise_or)\
                   .then_inc(signed, 1)

            def mask(g, c, h):
                m, t, a = piece(g, c, h)
                dve.wait_ge(expd, m + 1)
                dve.scalar_tensor_tensor(a, a, 1.0, t[:, :], ALU.is_lt, ALU.mult).then_inc(weighed, 1)

            def weigh(g, c, k, more):
                after = (g, c + 1) if c + 1 < CHUNKS else (g + 1, 0)
                if k < 2:
                    sign(g, c, k)
                elif k < 4 and more:
                    clamp(*after, k - 2)
                elif k == 5 or k == 7:
                    mask(g, c, (k - 5) // 2)

            for h in range(PIECES):
                clamp(0, 0, h)
            for k in range(KC):
                weigh(0, 0, k, True)

            def finish_result(n, k):
                if k == 4:
                    dve.wait_ge(acc_turned, SLABS + n + 1)
                    wait(dve, stored, 16 * n)
                    dve.tensor_tensor(result[:, :, :], xbank[:, :, :], of_slab(tokens, n), ALU.add)\
                       .then_inc(result_ready, 1)

            def slab(g, before, last):
                for k in range(KB):
                    c, kc = divmod(k, KC)
                    evacuate(1, g, k)
                    if not (last and c + 1 == CHUNKS):
                        after = (g, c + 1) if c + 1 < CHUNKS else (g + 1, 0)
                        weigh(*after, kc, not (last and c + 2 >= CHUNKS))
                    if before == "message":
                        finish_message(SLABS - 1, k)
                    else:
                        finish_result(g - 1, k)

            slab(0, "message", False)
            with dve.Fori(1, SLABS - 1) as g:
                slab(g, "result", False)
            slab(SLABS - 1, "result", True)
            finish_result(SLABS - 1, 4)


_INS = ['x', 'adj', 'L0_gnn_weight', 'L0_gnn_bias', 'L1_gnn_W', 'L1_gnn_B']
_OUTS = [((N, D), 'float32')]


def kernel(**inputs):
    import numpy as _np
    import concourse.bacc as _bacc
    from concourse import mybir as _mybir
    from concourse.bass_utils import run_bass_kernel_spmd as _run

    nc = _bacc.Bacc("TRN2", target_bir_lowering=False, num_devices=1)
    arrays, args = {}, []
    for name in _INS:
        a = _np.ascontiguousarray(inputs[name])
        arrays[f"in_{name}_dram"] = a
        args.append(nc.dram_tensor(f"in_{name}_dram", a.shape, _mybir.dt.from_np(a.dtype), kind="ExternalInput").ap())
    for i, (shape, dtype) in enumerate(_OUTS):
        dt = _mybir.dt.from_np(_np.dtype(dtype))
        args.append(nc.dram_tensor(f"out_{i}_dram", shape, dt, kind="ExternalOutput").ap())
    graph_layers(nc, *args)
    r = _run(nc, [arrays], core_ids=[0])
    return r.results[0]["out_0_dram"]
```

```python
import concourse.bass as bass
from concourse import mybir
from contextlib import ExitStack

P = 128
Q = 4
R = P // Q
N = 4096
D = 128
QCOLS = N // Q
KB = N // P
SUB = 4
SLAB = SUB * P
SLABS = N // SLAB
CHUNKS = 4
CCOLS = QCOLS // CHUNKS
KC = KB // CHUNKS
GROUPS = SLAB // R
ROW = GROUPS * CCOLS
PIECE = ROW // 2
PIECES = 4
EPS = 1e-5
TINY = 2.0 ** -60
LAYERS = 2


def graph_layers(nc, x, adj, w0, b0, w1, b1, out):
    f32 = mybir.dt.float32
    ALU, ACT, AX = mybir.AluOpType, mybir.ActivationFunctionType, mybir.AxisListType

    made = nc.dram_tensor("edge_weights", [SLABS, PIECES, P, PIECE], f32, kind="Internal").ap()
    sums_v = adj.rearrange("(q g t r) (c n) -> q g c r t n", q=Q, g=SLABS, t=SUB, c=CHUNKS)
    cols_v = adj.rearrange("(o g t r) (q c n) -> q o g c r t n", o=Q, g=SLABS, t=SUB, q=Q, c=CHUNKS)
    x_v = x.rearrange("(q t r) f -> q r t f", q=Q, r=R)
    out_v = out.rearrange("(q g t r) f -> q g r t f", q=Q, g=SLABS, t=SUB)

    ctx = ExitStack()
    with ctx:
        def sb(name, shape, dt=f32):
            return ctx.enter_context(nc.sbuf_tensor(name, shape, dt))

        def pb(name, shape):
            return ctx.enter_context(nc.psum_tensor(name, shape, f32))

        def sem(name):
            return ctx.enter_context(nc.semaphore(name))

        chunk = [sb(f"chunk{c}", [P, ROW]) for c in range(CHUNKS)]
        chunk_t = [sb(f"chunk_t{n}", [P, KC, SLAB]) for n in range(2)]
        odds = [sb(f"odds{n}", [P, PIECE]) for n in range(PIECES)]
        recip = [sb(f"recip{n}", [P, PIECE]) for n in range(2)]
        tokens = sb("tokens", [P, KB, D])
        support = sb("support", [P, KB, D])
        message = sb("message", [P, KB, D])
        weight = [sb("weight0", [P, D]), sb("weight1", [P, D])]
        bias = [sb("bias0", [P, D]), sb("bias1", [P, D])]
        ident = sb("ident", [P, P])
        tiny = sb("tiny", [P, 1])
        row_part = sb("row_part", [P, KB, CHUNKS])
        degree = sb("degree", [P, KB])
        dinv = sb("dinv", [P, KB])
        dtmp = sb("dtmp", [P, KB])
        dlog = sb("dlog", [P, KB])
        mean = sb("mean", [P, SUB])
        var = sb("var", [P, SUB])
        vlog = sb("vlog", [P, SUB])
        rstd = sb("rstd", [P, SUB])
        rtmp = sb("rtmp", [P, SUB])
        centred = sb("centred", [P, SUB, D])
        hidden = sb("hidden", [P, SUB, D])
        hidden_t = sb("hidden_t", [P, SLAB])
        acc_t = sb("acc_t", [P, SLAB])
        result = sb("result", [P, SUB, D])

        acc = pb("acc", [P, SLAB])
        hbank = pb("hbank", [P, SLAB])
        xbank = pb("xbank", [P, SUB, D])

        inputs_in = sem("inputs_in")
        loaded = [sem(f"loaded{c}") for c in range(CHUNKS)]
        constants = sem("constants")
        summed = sem("summed")
        dve_step = sem("dve_step")
        var_ready = sem("var_ready")
        rstd_seed = sem("rstd_seed")
        small_log = sem("small_log")
        hidden_ready = sem("hidden_ready")
        hidden_turned = sem("hidden_turned")
        hidden_t_ready = sem("hidden_t_ready")
        projected = sem("projected")
        support_raw = sem("support_raw")
        degree_ready = sem("degree_ready")
        dinv_seed = sem("dinv_seed")
        support_ready = sem("support_ready")
        bias_added = sem("bias_added")
        turned = sem("turned")
        multiplied = sem("multiplied")
        acc_out = sem("acc_out")
        acc_turned = sem("acc_turned")
        x1_kept = sem("x1_kept")
        message_ready = sem("message_ready")
        masked = sem("masked")
        complemented = sem("complemented")
        squared = sem("squared")
        ln_done = sem("ln_done")
        inverted = sem("inverted")
        divided = [sem(f"divided{r}") for r in range(PIECES)]
        weighed = sem("weighed")
        spilled = [sem(f"spilled{r}") for r in range(PIECES)]
        result_ready = sem("result_ready")
        stored = sem("stored")

        block = ctx.enter_context(nc.Block())

        LEAD = 3

        def started(turn, g, j):
            if turn == 0:
                return 0, g, j
            g, r = g + (j + LEAD) // PIECES, (j + LEAD) % PIECES
            return None if isinstance(g, int) and g >= SLABS else (1, g, r)

        def before(turn, g, j, lag):
            r = j - lag + (LEAD if turn else 0)
            g, r = g + r // PIECES, r % PIECES
            if isinstance(g, int) and g < 0:
                return (0, g + SLABS, r) if turn else None
            if isinstance(g, int) and g >= SLABS:
                return None
            return turn, g, r

        def number(piece):
            turn, g, r = piece
            return PIECES * (turn * SLABS + g) + r

        POOL_DIVIDES = ((0, 0), (0, 1), (0, 2))

        def wait_divided(eng, piece):
            turn, g, r = piece
            eng.wait_ge(divided[r], turn * SLABS + g + 1)

        def divide(eng, piece):
            r = piece[2]
            eng.wait_ge(inverted, number(piece) + 1)
            eng.tensor_tensor(odds[r][:, :], odds[r][:, :], recip[r % 2][:, :], ALU.mult).then_inc(divided[r], 1)

        def slot(piece):
            return 2 * (piece[2] // 2) + piece[0]

        def source(piece):
            h = piece[2] % 2
            return chunk[slot(piece)][:, h * PIECE:(h + 1) * PIECE]

        def wait(eng, s, value):
            if not isinstance(value, int) or value > 0:
                eng.wait_ge(s, value)

        def of_slab(t, g):
            return t[:, bass.ds(g * SUB, SUB)]

        def per_row(t):
            return t.unsqueeze(2).to_broadcast([P, SUB, D])

        def at(view, g, *rest):
            if isinstance(g, int):
                return view[(g,) + rest]
            return view[(bass.ds(g, 1),) + rest].squeeze(0)

        SUMS_LOAD, LOAD, MADE_LOAD = Q * 16, Q * Q * 16, 2 * 16
        HALVES = {"sp": (0, 2), "act": (1, 3)}

        def loads_before(turn):
            return SLABS * (SUMS_LOAD + turn * LOAD)

        def quarter(t, q):
            return t[q * R:(q + 1) * R]

        def load_for_sums(eng, who, g, c):
            for q in HALVES[who]:
                dst = quarter(chunk[c], q).rearrange("r (t n) -> r t n", t=SUB)
                eng.dma_start(dst, at(sums_v[q], g, c)).then_inc(loaded[c], 16)

        def load(eng, g, c):
            for o in range(Q):
                for q in (2, 0, 3, 1):
                    dst = quarter(chunk[c], q)[:, o * (ROW // Q):(o + 1) * (ROW // Q)]
                    eng.dma_start(dst.rearrange("r (t n) -> r t n", t=SUB), at(cols_v[q, o], g, c))\
                       .then_inc(loaded[c], 16)

        def slot_summed(eng, g, c):
            eng.wait_ge(summed, CHUNKS * g + c + 1)

        def slot_turned(eng, turn, g, c):
            eng.wait_ge(turned, CHUNKS * (turn * SLABS + g) + c + 1)

        def slot_used(eng, turn, g, r):
            eng.wait_ge(complemented, number((turn, g, r)) + 1)
            eng.wait_ge(squared, number((turn, g, r)) + 1)

        @block.sync
        def _(sp):
            for q in range(Q):
                sp.dma_start(quarter(tokens, q), x_v[q]).then_inc(inputs_in, 16)
            sp.dma_start(weight[0][:, :], w0).then_inc(inputs_in, 16)
            sp.dma_start(weight[1][:, :], w1).then_inc(inputs_in, 16)
            for n, b in enumerate((b0, b1)):
                sp.dma_start(bias[n][:, :], b.rearrange("(o f) -> o f", o=1).to_broadcast([P, D]))\
                  .then_inc(inputs_in, 16)

            for c in range(CHUNKS):
                load_for_sums(sp, "sp", 0, c)
            with sp.Fori(1, SLABS) as g:
                for c in range(CHUNKS):
                    slot_summed(sp, g - 1, c)
                    load_for_sums(sp, "sp", g, c)

            for c in range(CHUNKS):
                slot_summed(sp, SLABS - 1, c)
                load(sp, 0, c)
            with sp.Fori(1, SLABS) as g:
                slot_turned(sp, 0, g - 1, 1)
                load(sp, g, 1)
                slot_used(sp, 0, g - 1, 1)
                load(sp, g, 0)
                slot_turned(sp, 0, g - 1, 3)
                load(sp, g, 3)
                slot_used(sp, 0, g - 1, 3)
                load(sp, g, 2)

            def load_made(g, c):
                for r in (c, c + 1):
                    sp.wait_ge(spilled[r], 16 * (g + 1))
                    sp.dma_start(chunk[c][:, (r % 2) * PIECE:(r % 2 + 1) * PIECE], at(made, g, r))\
                      .then_inc(loaded[c], 16)

            slot_turned(sp, 0, SLABS - 1, 1)
            load(sp, 0, 1)
            slot_used(sp, 0, SLABS - 1, 1)
            load_made(0, 0)
            slot_turned(sp, 0, SLABS - 1, 3)
            load(sp, 0, 3)
            slot_used(sp, 0, SLABS - 1, 3)
            load_made(0, 2)
            slot_used(sp, 1, 0, 1)
            load(sp, 1, 1)

            def next_slab(g, more):
                slot_turned(sp, 1, g, 0)
                load_made(g + 1, 0)
                slot_used(sp, 1, g, 3)
                load(sp, g + 1, 3)
                slot_turned(sp, 1, g, 2)
                load_made(g + 1, 2)
                if more:
                    slot_used(sp, 1, g + 1, 1)
                    load(sp, g + 2, 1)

            next_slab(0, True)
            with sp.Fori(1, SLABS - 2) as g:
                next_slab(g, True)
            next_slab(SLABS - 2, False)

        @block.gpsimd
        def _(pool):
            pool.memset(tiny[:, :], TINY).then_inc(constants, 1)
            pool.memset(ident[:, :], 0.0).then_inc(constants, 1)
            pool.wait_ge(constants, 2)
            pool.affine_select(out=ident[:, :], in_=ident[:, :], compare_op=ALU.not_equal, fill=1.0, base=0,
                               pattern=[[-1, P]], channel_multiplier=1).then_inc(constants, 1)
            pool.wait_ge(inputs_in, 8 * 16)
            pool.wait_ge(hidden_ready, SLABS)
            pool.tensor_tensor(tokens[:, :, :], tokens[:, :, :],
                               bias[0][:, :].unsqueeze(1).to_broadcast([P, KB, D]), ALU.add).then_inc(bias_added, 1)

            def beat(turn, g, j):
                piece, last, other = started(turn, g, j), before(turn, g, j, 1), before(turn, g, j, 2)
                if piece:
                    a = source(piece)
                    pool.wait_ge(masked, number(piece) + 1)
                    if other:
                        wait_divided(pool, other)
                    pool.tensor_tensor(recip[piece[2] % 2][:, :], a, a, ALU.mult).then_inc(squared, 1)
                if last and (last[0], last[2]) in POOL_DIVIDES:
                    divide(pool, last)

            def beats(turn, g):
                for j in range(PIECES):
                    beat(turn, g, j)

            def store(g):
                pool.wait_ge(result_ready, g + 1)
                for q in range(Q):
                    pool.dma_start(at(out_v[q], g), quarter(result, q)).then_inc(stored, 16)

            beats(0, 0)
            with pool.Fori(1, SLABS) as g:
                beats(0, g)
            for j in range(-LEAD, 0):
                beat(1, 0, j)
            beats(1, 0)
            with pool.Fori(1, SLABS - 1) as g:
                beats(1, g)
                store(g - 1)
            beats(1, SLABS - 1)
            for g in range(SLABS - 2, SLABS):
                store(g)
            pool.wait_ge(stored, Q * 16 * SLABS)

        @block.tensor
        def _(pe):
            def turn_hidden(n):
                pe.wait_ge(hidden_ready, n + 1)
                wait(pe, hidden_t_ready, n)
                for s in range(SUB):
                    last = pe.transpose(hbank[:, bass.ts(s, P)], hidden[:, s, :], ident[:, :])
                last.then_inc(hidden_turned, 1)

            def project(n, w):
                pe.wait_ge(hidden_t_ready, n + 1)
                for s in range(SUB):
                    last = pe.matmul(xbank[:, s, :], hidden_t[:, bass.ts(s, P)], weight[w][:, :], start=True, stop=True)
                last.then_inc(projected, 1)

            def turn_acc(n):
                pe.wait_ge(acc_out, n + 1)
                for s in range(SUB):
                    last = pe.transpose(xbank[:, s, :], acc_t[:, bass.ts(s, P)], ident[:, :])
                last.then_inc(acc_turned, 1)

            def multiply(turn, g, k):
                c, kc = divmod(k, KC)
                if k == 0:
                    wait(pe, acc_out, turn * SLABS + g)
                if k % SUB == 0:
                    pe.wait_ge((support_ready, message_ready)[turn], k // SUB + 1)
                if kc == 0:
                    pe.wait_ge(turned, CHUNKS * (turn * SLABS + g) + c + 1)
                pe.matmul(acc[:, :], (support, message)[turn][:, k, :], chunk_t[c % 2][:, kc, :], start=k == 0,
                          stop=k == KB - 1).then_inc(multiplied, 1)

            def slab(turn, g, finish):
                n = turn * SLABS + g
                for k in range(KB):
                    if finish == "message" and k == 3 * KC:
                        project(SLABS + n - 1, 1)
                    multiply(turn, g, k)
                    if finish and k == 0:
                        if finish == "message":
                            pe.wait_ge(support_raw, SLABS)
                            wait(pe, message_ready, n - 1)
                        else:
                            pe.wait_ge(message_ready, SLABS)
                            wait(pe, result_ready, n - SLABS - 1)
                        turn_acc(n - 1)
                    if finish == "message" and k == 3 * KC - 2:
                        turn_hidden(SLABS + n - 1)

            pe.wait_ge(constants, 3)
            pe.wait_ge(inputs_in, 8 * 16)
            turn_hidden(0)
            project(0, 0)
            with pe.Fori(1, SLABS) as g:
                turn_hidden(g)
                pe.wait_ge(support_raw, g)
                project(g, 0)
            slab(0, 0, None)
            with pe.Fori(1, SLABS) as g:
                slab(0, g, "message")
            pe.wait_ge(message_ready, SLABS - 1)
            turn_acc(SLABS - 1)
            turn_hidden(2 * SLABS - 1)
            project(2 * SLABS - 1, 1)
            slab(1, 0, None)
            with pe.Fori(1, SLABS) as g:
                slab(1, g, "result")
            pe.wait_ge(result_ready, SLABS - 1)
            turn_acc(2 * SLABS - 1)

        @block.scalar
        def _(act):
            def norm_seed(n, step):
                act.wait_ge(var_ready, n + 1)
                act.activation(vlog[:, :], var[:, :], ACT.Ln).then_inc(small_log, 1)
                act.wait_ge(small_log, step + 1)
                act.activation(rstd[:, :], vlog[:, :], ACT.Exp, scale=-0.5).then_inc(rstd_seed, 1)

            def relu_hidden(n):
                act.wait_ge(hidden_turned, n + 1)
                wait(act, projected, n)
                act.activation(hidden_t[:, :], hbank[:, :], ACT.Relu).then_inc(hidden_t_ready, 1)

            def copy_acc(n):
                act.wait_ge(multiplied, KB * (n + 1))
                wait(act, acc_turned, n)
                act.activation(acc_t[:, :], acc[:, :], ACT.Copy).then_inc(acc_out, 1)

            def copy_support(g):
                act.wait_ge(projected, g + 1)
                act.activation(of_slab(support, g), xbank[:, :, :], ACT.Copy).then_inc(support_raw, 1)

            act.preload_act_table_set("natural_log_exp_and_others")
            for c in range(CHUNKS):
                load_for_sums(act, "act", 0, c)

            def pass1(g, load_next):
                norm_seed(g, g)
                for c in range(CHUNKS):
                    if c == 2:
                        relu_hidden(g)
                        copy_support(g)
                    if load_next:
                        slot_summed(act, g, c)
                        load_next(c)

            with act.Fori(0, SLABS - 1) as g:
                pass1(g, lambda c: load_for_sums(act, "act", g + 1, c))
            pass1(SLABS - 1, None)
            act.wait_ge(degree_ready, 1)
            act.activation(dlog[:, :], degree[:, :], ACT.Ln).then_inc(small_log, 1)
            act.wait_ge(small_log, SLABS + 1)
            act.activation(dinv[:, :], dlog[:, :], ACT.Exp, scale=-0.5).then_inc(dinv_seed, 1)

            def complement(piece):
                turn, g, r = piece
                act.wait_ge(masked, number(piece) + 1)
                last = before(turn, g, r, PIECES + (LEAD if turn else 0))
                if last and last[0] == 0:
                    act.wait_ge(spilled[r], 16 * (last[1] + 1))
                elif last:
                    slot_turned(act, 1, last[1], slot(last))
                act.activation(odds[r][:, :], source(piece), ACT.Square, bias=1.0, scale=-1.0)\
                   .then_inc(complemented, 1)

            def log(piece):
                t = recip[piece[2] % 2]
                act.wait_ge(squared, number(piece) + 1)
                act.activation(t[:, :], t[:, :], ACT.Ln, bias=tiny[:, :]).then_inc(ln_done, 1)

            def invert(piece):
                t = recip[piece[2] % 2]
                act.wait_ge(ln_done, number(piece) + 1)
                act.activation(t[:, :], t[:, :], ACT.Exp, scale=-1.0).then_inc(inverted, 1)

            def gaussian(piece):
                t = odds[piece[2]]
                wait_divided(act, piece)
                act.activation(t[:, :], t[:, :], ACT.Exp, scale=-2.0).then_inc(weighed, 1)

            def spill(piece):
                turn, g, r = piece
                act.wait_ge(weighed, number(piece) + 1)
                act.dma_start(at(made, g, r), odds[r][:, :]).then_inc(spilled[r], 16)

            def beat(turn, g, j, norm=None, relu=None, acc_done=None):
                p1, p2, p3 = (before(turn, g, j, lag) for lag in (1, 2, 3))
                if norm is not None:
                    norm_seed(*norm)
                if p1:
                    complement(p1)
                if relu is not None:
                    relu_hidden(relu)
                if p3 and p3[0] == 0:
                    spill(p3)
                if p1:
                    log(p1)
                if acc_done is not None:
                    copy_acc(acc_done)
                if p1:
                    invert(p1)
                if p2:
                    gaussian(p2)

            def slab(turn, g, finish):
                n = turn * SLABS + g
                for j in range(PIECES):
                    message = finish == "message"
                    beat(turn, g, j,
                         norm=(SLABS + n - 1, SLABS + n) if message and j == 2 else None,
                         relu=SLABS + n - 1 if message and j == 3 else None,
                         acc_done=n - 1 if finish and j == 0 else None)
            slab(0, 0, None)
            with act.Fori(1, SLABS) as g:
                slab(0, g, "message")

            n = SLABS - 1
            beat(1, 0, -3, acc_done=n)
            beat(1, 0, -2)
            beat(1, 0, -1, norm=(SLABS + n, SLABS + n + 1))
            relu_hidden(SLABS + n)

            slab(1, 0, None)
            with act.Fori(1, SLABS - 1) as g:
                slab(1, g, "result")
            slab(1, SLABS - 1, "result")
            copy_acc(2 * SLABS - 1)

        @block.vector
        def _(dve):
            NORM_STEPS = 9
            MIX_STEPS = 3
            DEGREE_STEPS = 5

            def link(base, j, ins):
                ins.then_inc(dve_step, 1)
                dve.wait_ge(dve_step, base + j)

            def norm_var(base, n, rows):
                link(base, 1, dve.reduce_sum(mean[:, :], rows, axis=AX.X))
                link(base, 2, dve.tensor_scalar(mean[:, :], mean[:, :], 1.0 / D, None, ALU.mult))
                link(base, 3, dve.tensor_tensor(centred[:, :, :], rows, per_row(mean[:, :]), ALU.subtract))
                wait(dve, hidden_turned, n)
                link(base, 4, dve.tensor_tensor(hidden[:, :, :], centred[:, :, :], centred[:, :, :], ALU.mult))
                link(base, 5, dve.reduce_sum(var[:, :], hidden[:, :, :], axis=AX.X))
                dve.tensor_scalar(var[:, :], var[:, :], 1.0 / D, EPS, ALU.mult, ALU.add).then_inc(var_ready, 1)

            def norm_out(base, n):
                dve.wait_ge(rstd_seed, n + 1)
                link(base, 6, dve.tensor_tensor(rtmp[:, :], rstd[:, :], rstd[:, :], ALU.mult))
                link(base, 7, dve.tensor_tensor(rtmp[:, :], rtmp[:, :], var[:, :], ALU.mult))
                link(base, 8, dve.tensor_scalar(rtmp[:, :], rtmp[:, :], -0.5, 1.5, ALU.mult, ALU.add))
                link(base, 9, dve.tensor_tensor(rstd[:, :], rstd[:, :], rtmp[:, :], ALU.mult))
                dve.tensor_tensor(hidden[:, :, :], centred[:, :, :], per_row(rstd[:, :]), ALU.mult)\
                   .then_inc(hidden_ready, 1)

            def row_sums(g, c):
                dve.wait_ge(loaded[c], SUMS_LOAD * (g + 1))
                dve.reduce_sum(row_part[:, bass.ds(g * SUB, SUB), c], chunk[c][:, :].rearrange("p (t n) -> p t n", t=SUB),
                               axis=AX.X).then_inc(summed, 1)

            dve.wait_ge(inputs_in, 8 * 16)

            def pass1(g):
                base = NORM_STEPS * g
                norm_var(base, g, of_slab(tokens, g))
                row_sums(g, 0)
                row_sums(g, 1)
                norm_out(base, g)
                row_sums(g, 2)
                row_sums(g, 3)

            pass1(0)
            with dve.Fori(1, SLABS) as g:
                pass1(g)
            base = NORM_STEPS * SLABS
            dve.wait_ge(summed, CHUNKS * SLABS)
            link(base, 1, dve.reduce_sum(degree[:, :], row_part[:, :, :], axis=AX.X))
            dve.tensor_scalar(degree[:, :], degree[:, :], 1.0, None, ALU.add).then_inc(degree_ready, 1)
            dve.wait_ge(dinv_seed, 1)
            link(base, 2, dve.tensor_tensor(dtmp[:, :], dinv[:, :], dinv[:, :], ALU.mult))
            link(base, 3, dve.tensor_tensor(dtmp[:, :], dtmp[:, :], degree[:, :], ALU.mult))
            link(base, 4, dve.tensor_scalar(dtmp[:, :], dtmp[:, :], -0.5, 1.5, ALU.mult, ALU.add))
            link(base, 5, dve.tensor_tensor(dinv[:, :], dinv[:, :], dtmp[:, :], ALU.mult))
            dve.wait_ge(support_raw, SLABS)
            for g in range(SLABS):
                dve.tensor_tensor(of_slab(support, g), of_slab(support, g), per_row(of_slab(dinv, g)), ALU.mult)\
                   .then_inc(support_ready, 1)
            PASS2 = base + DEGREE_STEPS
            dve.wait_ge(support_ready, SLABS)
            dve.wait_ge(bias_added, 1)

            def turn_chunk(turn, g, c):
                n = CHUNKS * (turn * SLABS + g) + c
                made_here = turn == 1 and c % 2 == 1
                if made_here:
                    dve.wait_ge(weighed, number((1, g, c)) + 1)
                else:
                    each = MADE_LOAD if turn == 1 else LOAD
                    dve.wait_ge(loaded[c], loads_before(turn) + each * (g + 1))
                wait(dve, multiplied, KC * (n - 1))
                for o in range(Q):
                    if made_here:
                        src = odds[c - 1 + o // 2][:, (o % 2) * (PIECE // 2):(o % 2 + 1) * (PIECE // 2)]
                    else:
                        src = chunk[c][:, o * (ROW // Q):(o + 1) * (ROW // Q)]
                    dst = chunk_t[c % 2][:, :, :].rearrange("p k (t o r) -> p o t k r", t=SUB, o=Q)[:, o]
                    last = dve.transpose(dst, src.rearrange("p (t k r) -> p t k r", t=SUB, k=KC))
                last.then_inc(turned, 1)

            def mask(piece):
                turn, g, r = piece
                if turn == 0:
                    slot_turned(dve, 0, g, slot(piece))
                elif r % 2 == 0:
                    dve.wait_ge(loaded[slot(piece)], loads_before(1) + LOAD * (g + 1))
                a = source(piece)
                dve.scalar_tensor_tensor(a, a, 1.0, a, ALU.is_lt, ALU.mult).then_inc(masked, 1)

            def mix(n):
                base = PASS2 + (MIX_STEPS + NORM_STEPS) * n
                dve.wait_ge(acc_turned, n + 1)
                link(base, 1, dve.tensor_tensor(centred[:, :, :], xbank[:, :, :], of_slab(support, n), ALU.add))
                link(base, 2, dve.tensor_tensor(centred[:, :, :], centred[:, :, :], per_row(of_slab(dinv, n)), ALU.mult))
                link(base, 3, dve.tensor_tensor(result[:, :, :], of_slab(tokens, n), centred[:, :, :], ALU.add))
                norm_var(base + MIX_STEPS, SLABS + n, result[:, :, :])
                dve.tensor_copy(of_slab(tokens, n), result[:, :, :]).then_inc(x1_kept, 1)

            def give_message(n):
                dve.wait_ge(projected, SLABS + n + 1)
                dve.tensor_tensor(of_slab(message, n), xbank[:, :, :],
                                  bias[1][:, :].unsqueeze(1).to_broadcast([P, SUB, D]), ALU.add)\
                   .then_inc(message_ready, 1)

            def give_result(n):
                dve.wait_ge(acc_turned, SLABS + n + 1)
                wait(dve, stored, Q * 16 * n)
                dve.tensor_tensor(result[:, :, :], xbank[:, :, :], of_slab(tokens, n), ALU.add)\
                   .then_inc(result_ready, 1)

            def beat(turn, g, j, chunk_too=True):
                if chunk_too:
                    turn_chunk(turn, g, j)
                if started(turn, g, j):
                    mask(started(turn, g, j))

            def end_beat(turn, g, j):
                last = before(turn, g, j, 1)
                if last and (last[0], last[2]) not in POOL_DIVIDES:
                    divide(dve, last)

            def slab(turn, g, finish):
                n = g - 1
                for j in range(CHUNKS):
                    beat(turn, g, j)
                    if finish == "message" and j == 1:
                        mix(n)
                    if finish == "message" and j == 2:
                        norm_out(PASS2 + (MIX_STEPS + NORM_STEPS) * n + MIX_STEPS, SLABS + n)
                    if finish == "result" and j == 1:
                        give_result(n)
                    end_beat(turn, g, j)
                    if finish == "message" and j == 3:
                        give_message(n)

            slab(0, 0, None)
            with dve.Fori(1, SLABS) as g:
                slab(0, g, "message")
            n = SLABS - 1
            for j in range(-LEAD, 0):
                mask((1, 0, j + LEAD))
                if j == -2:
                    mix(n)
                if j == -1:
                    norm_out(PASS2 + (MIX_STEPS + NORM_STEPS) * n + MIX_STEPS, SLABS + n)
                end_beat(1, 0, j)
            beat(1, 0, 0)
            give_message(n)
            end_beat(1, 0, 0)
            for j in range(1, CHUNKS):
                beat(1, 0, j)
                end_beat(1, 0, j)
            dve.wait_ge(x1_kept, SLABS)
            with dve.Fori(1, SLABS - 1) as g:
                slab(1, g, "result")
            slab(1, SLABS - 1, "result")
            give_result(SLABS - 1)


_INS = ['x', 'adj', 'L0_gnn_weight', 'L0_gnn_bias', 'L1_gnn_W', 'L1_gnn_B']
_OUTS = [((N, D), 'float32')]


def kernel(**inputs):
    import numpy as _np
    import concourse.bacc as _bacc
    from concourse import mybir as _mybir
    from concourse.bass_utils import run_bass_kernel_spmd as _run

    nc = _bacc.Bacc("TRN2", target_bir_lowering=False, num_devices=1)
    arrays, args = {}, []
    for name in _INS:
        a = _np.ascontiguousarray(inputs[name])
        arrays[f"in_{name}_dram"] = a
        args.append(nc.dram_tensor(f"in_{name}_dram", a.shape, _mybir.dt.from_np(a.dtype), kind="ExternalInput").ap())
    for i, (shape, dtype) in enumerate(_OUTS):
        dt = _mybir.dt.from_np(_np.dtype(dtype))
        args.append(nc.dram_tensor(f"out_{i}_dram", shape, dt, kind="ExternalOutput").ap())
    graph_layers(nc, *args)
    r = _run(nc, [arrays], core_ids=[0])
    return r.results[0]["out_0_dram"]
```

```python
import concourse.bass as bass
from concourse import mybir
from contextlib import ExitStack

P = 128
Q = 4
R = P // Q
N = 4096
D = 128
QCOLS = N // Q
KB = N // P
SUB = 4
SLAB = SUB * P
SLABS = N // SLAB
CHUNKS = 4
CCOLS = QCOLS // CHUNKS
KC = KB // CHUNKS
PARTS = 2
KP = KC // PARTS
GROUPS = SLAB // R
ROW = GROUPS * CCOLS
PIECE = ROW // 2
PASSES = 3
MADE_IN = (((3, 1), (1, 1)), ((0, 1), (1, 0), (2, 1)), ((0, 0), (2, 0), (3, 0)))
BUFFERS = 3
KEPT = MADE_IN[0] + MADE_IN[1]
EPS = 1e-5
TINY = 2.0 ** -60


def graph_layers(nc, x, adj, w0, b0, w1, b1, out):
    f32 = mybir.dt.float32
    ALU, ACT, AX = mybir.AluOpType, mybir.ActivationFunctionType, mybir.AxisListType

    made = nc.dram_tensor("edge_weights", [SLABS, 1 + len(KEPT), P, PIECE], f32, kind="Internal").ap()
    made_at = {half: 1 + i for i, half in enumerate(KEPT)}
    cols_v = adj.rearrange("(s g r) (q c n) -> q g c r s n", g=SLABS, r=R, q=Q, c=CHUNKS)
    x_v = x.rearrange("(q t r) f -> q r t f", q=Q, r=R)
    out_v = out.rearrange("(q t g r) f -> q g r t f", q=Q, g=SLABS, t=SUB)

    ctx = ExitStack()
    with ctx:
        def sb(name, shape, dt=f32):
            return ctx.enter_context(nc.sbuf_tensor(name, shape, dt))

        def pb(name, shape):
            return ctx.enter_context(nc.psum_tensor(name, shape, f32))

        def sem(name):
            return ctx.enter_context(nc.semaphore(name))

        chunk = [sb(f"chunk{c}", [P, ROW]) for c in range(CHUNKS)]
        chunk_t = [sb(f"chunk_t{n}", [P, KC, SLAB]) for n in range(2)]
        odds = [sb(f"odds{n}", [P, PIECE]) for n in range(BUFFERS)]
        recip = [sb(f"recip{n}", [P, PIECE]) for n in range(BUFFERS)]
        tokens = sb("tokens", [P, KB, D])
        support = sb("support", [P, KB, D])
        message = sb("message", [P, KB, D])
        weight = [sb("weight0", [P, D]), sb("weight1", [P, D])]
        bias = [sb("bias0", [P, D]), sb("bias1", [P, D])]
        ident = sb("ident", [P, P])
        tiny = sb("tiny", [P, 1])
        fold = message[:, 0:Q, :]
        row_part = message[:, Q:2 * Q, :].rearrange("p c (g s) -> p c g s", g=SLABS)
        row_sum = message[:, 2 * Q, :]
        degree = sb("degree", [P, KB])
        dinv = sb("dinv", [P, KB])
        dtmp = sb("dtmp", [P, KB])
        dlog = sb("dlog", [P, KB])
        stats = sb("stats", [P, SUB, 6])
        gap = sb("gap", [P, SUB])
        squares = sb("squares", [P, SUB])
        mean2 = sb("mean2", [P, SUB])
        var = sb("var", [P, SUB])
        vlog = sb("vlog", [P, SUB])
        rstd = sb("rstd", [P, SUB])
        rtmp = sb("rtmp", [P, SUB])
        centred = sb("centred", [P, SUB, D])
        hidden = sb("hidden", [P, SUB, D])
        hidden_t = sb("hidden_t", [P, SLAB])
        acc_t = sb("acc_t", [P, SLAB])
        result = sb("result", [P, SUB, D])

        acc = pb("acc", [P, SLAB])
        hbank = pb("hbank", [P, SLAB])
        xbank = pb("xbank", [P, SUB, D])

        inputs_in = sem("inputs_in")
        loaded = [[sem(f"loaded{c}_{h}") for h in range(2)] for c in range(CHUNKS)]
        constants = sem("constants")
        summed = sem("summed")
        parts_added = sem("parts_added")
        folded = sem("folded")
        dve_step = sem("dve_step")
        var_ready = sem("var_ready")
        rstd_seed = sem("rstd_seed")
        small_log = sem("small_log")
        hidden_ready = sem("hidden_ready")
        hidden_turned = sem("hidden_turned")
        hidden_t_ready = sem("hidden_t_ready")
        projected = sem("projected")
        support_raw = sem("support_raw")
        degree_ready = sem("degree_ready")
        dinv_seed = sem("dinv_seed")
        support_ready = sem("support_ready")
        bias_added = sem("bias_added")
        turned = sem("turned")
        multiplied = sem("multiplied")
        acc_out = sem("acc_out")
        acc_turned = sem("acc_turned")
        x1_kept = sem("x1_kept")
        message_ready = sem("message_ready")
        masked = sem("masked")
        complemented = sem("complemented")
        squared = sem("squared")
        ln_done = sem("ln_done")
        inverted = sem("inverted")
        divided = [sem(f"divided{r}") for r in range(BUFFERS)]
        weighed = sem("weighed")
        spilled = [sem(f"spilled{r}") for r in range(BUFFERS)]
        result_ready = sem("result_ready")
        stored = sem("stored")

        block = ctx.enter_context(nc.Block())

        def pieces(t):
            return len(MADE_IN[t])

        def number(piece):
            t, g, r = piece
            return SLABS * sum(pieces(u) for u in range(t)) + pieces(t) * g + r

        def before(t, g, j, lag):
            g, r = g + (t == PASSES - 1) + (j - lag) // pieces(t), (j - lag) % pieces(t)
            if not isinstance(g, int) or 0 <= g < SLABS:
                return t, g, r
            if g >= SLABS or t == 1:
                return None
            return 1, SLABS + g, r

        def started(t, g, j):
            return before(t, g, j, 0)

        def uses(piece):
            t, g, r = piece
            return g + 1 + SLABS * sum(r < pieces(u) for u in range(t))

        def previous(piece):
            t, g, r = piece
            if not isinstance(g, int) or g > 0:
                return t, g - 1, r
            if t == 0 or r >= pieces(t - 1) and t == 1:
                return None
            return t - 1, SLABS - 1, r

        def slab_of(t, g):
            if t != 1:
                return g
            return SLABS - 1 if isinstance(g, int) and g == 0 else g - 1

        POOL_DIVIDES = ((0, 1), (1, 0), (1, 1), (1, 2), (2, 1), (2, 2))

        def wait_divided(eng, piece):
            eng.wait_ge(divided[piece[2]], uses(piece))

        def wait_spilled(eng, piece):
            eng.wait_ge(spilled[piece[2]], 16 * uses(piece))

        def divide(eng, piece):
            r = piece[2]
            eng.wait_ge(inverted, number(piece) + 1)
            eng.wait_ge(complemented, number(piece) + 1)
            eng.tensor_tensor(odds[r][:, :], odds[r][:, :], recip[r][:, :], ALU.mult).then_inc(divided[r], 1)

        def source(piece):
            c, h = MADE_IN[piece[0]][piece[2]]
            return chunk[c][:, h * PIECE:(h + 1) * PIECE]

        def wait(eng, s, value):
            if not isinstance(value, int) or value > 0:
                eng.wait_ge(s, value)

        def of_slab(t, g):
            tiles = t.rearrange("p (t g) ... -> p g t ...", g=SLABS)
            return tiles[:, g] if isinstance(g, int) else tiles[:, bass.ds(g, 1)].squeeze(1)

        def per_row(t):
            return t.unsqueeze(2).to_broadcast([P, SUB, D])

        def at(view, g, *rest):
            if isinstance(g, int):
                return view[(g,) + rest]
            return view[(bass.ds(g, 1),) + rest].squeeze(0)

        LOAD, KEPT_LOAD = Q * 16, 16

        def quarter(t, q):
            return t[q * R:(q + 1) * R]

        def load(t, g, c, h):
            half = chunk[c][:, h * PIECE:(h + 1) * PIECE]
            if t == PASSES - 1 and (c, h) in KEPT:
                i = KEPT.index((c, h))
                if i < pieces(0):
                    wait_spilled(nc.sync, (0, g, i))
                else:
                    last = isinstance(g, int) and g == SLABS - 1
                    wait_spilled(nc.sync, (1, 0 if last else g + 1, i - pieces(0)))
                nc.sync.dma_start(half, at(made, g, made_at[c, h])).then_inc(loaded[c][h], 16)
                return
            for q in (2, 0, 3, 1):
                dst = quarter(half, q).rearrange("r (s n) -> r s n", n=CCOLS)
                src = at(cols_v[q], slab_of(t, g), c, slice(None), slice(h * GROUPS // 2, (h + 1) * GROUPS // 2))
                nc.sync.dma_start(dst, src).then_inc(loaded[c][h], 16)

        def wait_loaded(eng, t, g, c, h):
            each = KEPT_LOAD if t == PASSES - 1 and (c, h) in KEPT else LOAD
            eng.wait_ge(loaded[c][h], LOAD * (SLABS * t - (t > 0)) + each * (g + 1))

        SUM_ORDER = (0, 3, 1, 2)

        def slot_summed(eng, g, c):
            eng.wait_ge(summed, CHUNKS * g + SUM_ORDER.index(c) + 1)

        def slot_turned(eng, t, g, c):
            eng.wait_ge(turned, PARTS * (CHUNKS * ((t - 1) * SLABS + g) + c + 1))

        def slot_masked(eng, piece):
            eng.wait_ge(masked, number(piece) + 1)

        @block.sync
        def _(sp):
            def load_inputs():
                for q in range(Q):
                    sp.dma_start(quarter(tokens, q), x_v[q]).then_inc(inputs_in, 16)
                sp.dma_start(weight[0][:, :], w0).then_inc(inputs_in, 16)
                sp.dma_start(weight[1][:, :], w1).then_inc(inputs_in, 16)
                for n, b in enumerate((b0, b1)):
                    sp.dma_start(bias[n][:, :], b.rearrange("(o f) -> o f", o=1).to_broadcast([P, D]))\
                      .then_inc(inputs_in, 16)

            for n, c in enumerate(SUM_ORDER):
                load(0, 0, c, 0)
                load(0, 0, c, 1)
                if n == 0:
                    load_inputs()

            def after_sums(g):
                slot_summed(sp, g, 0)
                load(0, g + 1, 0, 0)
                load(0, g + 1, 0, 1)
                slot_masked(sp, (0, g, 0))
                load(0, g + 1, 3, 0)
                load(0, g + 1, 3, 1)
                slot_masked(sp, (0, g, 1))
                load(0, g + 1, 1, 0)
                load(0, g + 1, 1, 1)
                slot_summed(sp, g, 2)
                load(0, g + 1, 2, 0)
                load(0, g + 1, 2, 1)

            def after_first(g, t, to):
                for c in range(CHUNKS):
                    slot_turned(sp, 1, g, c)
                    if c == 3:
                        load(t, to, c, 0)
                        load(t, to, c, 1)
                    else:
                        made_h = MADE_IN[1][c][1]
                        load(t, to, c, 1 - made_h)
                        slot_masked(sp, (1, g, c))
                        load(t, to, c, made_h)

            def store(g):
                sp.wait_ge(result_ready, g + 1)
                for q in range(Q):
                    sp.dma_start(at(out_v[q], g), quarter(result, q)).then_inc(stored, 16)

            def after_second(g):
                inside = not isinstance(g, int)
                for r, c in enumerate((0, 2, 3)):
                    if inside or 0 <= g < SLABS - 1:
                        slot_turned(sp, 2, g, c)
                        load(2, g + 1, c, 1)
                    if inside or g < SLABS - 2:
                        slot_masked(sp, (2, g + 1, r))
                        load(2, g + 2, c, 0)
                    if r == 0 and (inside or 0 <= g < SLABS - 1):
                        slot_turned(sp, 2, g, 1)
                        load(2, g + 1, 1, 0)
                        load(2, g + 1, 1, 1)

            with sp.Fori(0, SLABS - 1) as g:
                after_sums(g)
            with sp.Fori(0, SLABS - 1) as g:
                after_first(g, 1, g + 1)
            after_first(SLABS - 1, 2, 0)
            after_second(-1)
            after_second(0)
            with sp.Fori(1, SLABS - 2) as g:
                after_second(g)
                store(g - 1)
            after_second(SLABS - 2)
            for g in range(SLABS - 3, SLABS):
                store(g)
            sp.wait_ge(stored, Q * 16 * SLABS)

        @block.gpsimd
        def _(pool):
            pool.memset(tiny[:, :], TINY).then_inc(constants, 1)
            pool.memset(ident[:, :], 0.0).then_inc(constants, 1)
            pool.wait_ge(constants, 2)
            pool.affine_select(out=ident[:, :], in_=ident[:, :], compare_op=ALU.not_equal, fill=1.0, base=0,
                               pattern=[[-1, P]], channel_multiplier=1).then_inc(constants, 1)
            pool.memset(fold[:, :, :], 0.0).then_inc(constants, 1)
            pool.wait_ge(constants, 4)
            for q in range(Q):
                pool.affine_select(out=fold[:, 0, 0:R], in_=fold[:, 0, 0:R], compare_op=ALU.not_equal, fill=1.0,
                                   base=-q * R, pattern=[[-1, R]], channel_multiplier=1).then_inc(constants, 1)
                pool.wait_ge(constants, 5 + q)
            for o in range(1, Q):
                pool.tensor_copy(fold[:, o, o * R:(o + 1) * R], fold[:, 0, 0:R]).then_inc(constants, 1)

            def square(piece):
                a = odds[piece[2]][:, :]
                pool.wait_ge(masked, number(piece) + 1)
                if previous(piece):
                    wait_divided(pool, previous(piece))
                pool.tensor_tensor(recip[piece[2]][:, :], a, a, ALU.mult).then_inc(squared, 1)

            def beat(turn, g, j):
                piece, last = started(turn, g, j), before(turn, g, j, 1)
                if piece:
                    square(piece)
                if last and (last[0], last[2]) in POOL_DIVIDES:
                    divide(pool, last)

            def beats(turn, g):
                for j in range(pieces(turn)):
                    beat(turn, g, j)

            def pass1(g):
                for j in range(pieces(0)):
                    square((0, g, j))
                for j in range(pieces(0)):
                    if (0, j) in POOL_DIVIDES:
                        divide(pool, (0, g, j))

            pass1(0)
            with pool.Fori(1, SLABS) as g:
                pass1(g)
            pool.wait_ge(inputs_in, 8 * 16)
            pool.wait_ge(hidden_ready, SLABS)
            pool.tensor_tensor(tokens[:, :, :], tokens[:, :, :],
                               bias[0][:, :].unsqueeze(1).to_broadcast([P, KB, D]), ALU.add).then_inc(bias_added, 1)
            beats(1, 0)
            with pool.Fori(1, SLABS) as g:
                beats(1, g)
            beats(2, -1)
            with pool.Fori(0, SLABS - 1) as g:
                beats(2, g)
            beats(2, SLABS - 1)

        @block.tensor
        def _(pe):
            def turn_hidden(n):
                pe.wait_ge(hidden_ready, n + 1)
                wait(pe, hidden_t_ready, n)
                for s in range(SUB):
                    last = pe.transpose(hbank[:, bass.ts(s, P)], hidden[:, s, :], ident[:, :])
                last.then_inc(hidden_turned, 1)

            def project(n, w):
                pe.wait_ge(hidden_t_ready, n + 1)
                for s in range(SUB):
                    last = pe.matmul(xbank[:, s, :], hidden_t[:, bass.ts(s, P)], weight[w][:, :], start=True, stop=True)
                last.then_inc(projected, 1)

            def turn_acc(n):
                pe.wait_ge(acc_out, n + 1)
                for s in range(SUB):
                    last = pe.transpose(xbank[:, s, :], acc_t[:, bass.ts(s, P)], ident[:, :])
                last.then_inc(acc_turned, 1)

            def multiply(turn, g, k):
                c, kc = divmod(k, KC)
                if k == 0:
                    if turn == 0 and isinstance(g, int) and g == 0:
                        pe.wait_ge(degree_ready, 1)
                    wait(pe, acc_out, turn * SLABS + g)
                    if turn == 1:
                        pe.wait_ge(message_ready, SLABS)
                if turn == 0 and k % SUB == 0:
                    pe.wait_ge(support_ready, k // SUB + 1)
                if kc % KP == 0:
                    pe.wait_ge(turned, PARTS * (CHUNKS * (turn * SLABS + g) + c) + kc // KP + 1)
                pe.matmul(acc[:, :], (support, message)[turn][:, k, :], chunk_t[c % 2][:, kc, :], start=k == 0,
                          stop=k == KB - 1).then_inc(multiplied, 1)

            def slab(turn, g, finish):
                n = turn * SLABS + g
                for k in range(KB):
                    if finish == "message" and k == 3 * KC:
                        project(SLABS + n - 1, 1)
                    multiply(turn, g, k)
                    if finish and k == 0:
                        if finish == "message":
                            pe.wait_ge(support_raw, SLABS)
                            wait(pe, message_ready, n - 1)
                        else:
                            pe.wait_ge(message_ready, SLABS)
                            wait(pe, result_ready, n - SLABS - 1)
                        turn_acc(n - 1)
                    if finish == "message" and k == 2 * KC + 2:
                        turn_hidden(SLABS + n - 1)

            pe.wait_ge(constants, 8 + Q - 1)
            pe.wait_ge(inputs_in, 8 * 16)
            turn_hidden(0)
            project(0, 0)
            with pe.Fori(1, SLABS) as g:
                turn_hidden(g)
                pe.wait_ge(support_raw, g)
                project(g, 0)
            pe.wait_ge(parts_added, 1)
            for o in range(Q):
                last = pe.matmul(acc[:, 0:KB], fold[:, o, :], row_sum.rearrange("p (g o t) -> p o t g", o=Q, t=SUB)[:, o],
                                 start=o == 0, stop=o == Q - 1)
            last.then_inc(folded, 1)
            slab(0, 0, None)
            with pe.Fori(1, SLABS) as g:
                slab(0, g, "message")
            pe.wait_ge(message_ready, SLABS - 1)
            turn_acc(SLABS - 1)
            turn_hidden(2 * SLABS - 1)
            project(2 * SLABS - 1, 1)
            slab(1, 0, None)
            with pe.Fori(1, SLABS) as g:
                slab(1, g, "result")
            pe.wait_ge(result_ready, SLABS - 1)
            turn_acc(2 * SLABS - 1)

        @block.scalar
        def _(act):
            def norm_seed(n, step):
                act.wait_ge(var_ready, n + 1)
                act.activation(vlog[:, :], var[:, :], ACT.Ln).then_inc(small_log, 1)
                act.wait_ge(small_log, step + 1)
                act.activation(rstd[:, :], vlog[:, :], ACT.Exp, scale=-0.5).then_inc(rstd_seed, 1)

            def relu_hidden(n):
                act.wait_ge(hidden_turned, n + 1)
                wait(act, projected, n)
                act.activation(hidden_t[:, :], hbank[:, :], ACT.Relu).then_inc(hidden_t_ready, 1)

            def copy_acc(n):
                act.wait_ge(multiplied, KB * (n + 1))
                wait(act, acc_turned, n)
                act.activation(acc_t[:, :].rearrange("p (t o r) -> p o t r", o=Q, t=SUB),
                               acc[:, :].rearrange("p (o t r) -> p o t r", o=Q, t=SUB), ACT.Copy).then_inc(acc_out, 1)

            def copy_support(g):
                act.wait_ge(projected, g + 1)
                act.activation(of_slab(support, g), xbank[:, :, :], ACT.Copy).then_inc(support_raw, 1)

            act.preload_act_table_set("natural_log_exp_and_others")

            def complement(piece):
                t = odds[piece[2]]
                act.wait_ge(squared, number(piece) + 1)
                act.activation(t[:, :], t[:, :], ACT.Square, bias=1.0, scale=-1.0).then_inc(complemented, 1)

            def log(piece):
                t = recip[piece[2]]
                act.wait_ge(squared, number(piece) + 1)
                act.activation(t[:, :], t[:, :], ACT.Ln, bias=tiny[:, :]).then_inc(ln_done, 1)

            def invert(piece):
                t = recip[piece[2]]
                act.wait_ge(ln_done, number(piece) + 1)
                act.activation(t[:, :], t[:, :], ACT.Exp, scale=-1.0).then_inc(inverted, 1)

            def gaussian(piece):
                t = odds[piece[2]]
                wait_divided(act, piece)
                act.activation(t[:, :], t[:, :], ACT.Exp, scale=-2.0).then_inc(weighed, 1)

            def spill(piece):
                turn, g, r = piece
                act.wait_ge(weighed, number(piece) + 1)
                act.dma_start(at(made, slab_of(turn, g), made_at[MADE_IN[turn][r]]), odds[r][:, :]).then_inc(spilled[r], 16)

            def beat(t, g, j, after={}, gaussian_first=False):
                p1, p2, p3 = (before(t, g, j, lag) for lag in (1, 2, 3))
                if p3 and p3[0] < 2:
                    spill(p3)
                steps = ((log, p1), (invert, p1), (complement, p1), (gaussian, p2))
                for step, piece in (steps[3:] + steps[:3] if gaussian_first else steps):
                    if piece:
                        step(piece)
                    if step in after:
                        after[step]()

            def pass1(g):
                first, second = (0, g, 0), (0, g, 1)
                norm_seed(g, g)
                log(first)
                invert(first)
                complement(first)
                log(second)
                invert(second)
                complement(second)
                gaussian(first)
                relu_hidden(g)
                spill(first)
                gaussian(second)
                copy_support(g)
                spill(second)

            with act.Fori(0, SLABS) as g:
                pass1(g)
            act.wait_ge(degree_ready, 1)
            act.activation(dlog[:, :], degree[:, :], ACT.Ln).then_inc(small_log, 1)
            act.wait_ge(small_log, SLABS + 1)
            act.activation(dinv[:, :], dlog[:, :], ACT.Exp, scale=-0.5).then_inc(dinv_seed, 1)

            def slab(t, g, done):
                last_message = isinstance(g, int) and g < 0
                n = SLABS - 1 if last_message else (t - 1) * SLABS + g - 1
                after = {j: {} for j in range(pieces(t))}
                if "sum" in done:
                    after[0][log if t == 2 and not last_message else complement] = lambda: copy_acc(n)
                if "norm" in done:
                    after[1][complement] = lambda: norm_seed(SLABS + n, SLABS + n + 1)
                    after[1 if last_message else 2][gaussian if last_message else complement] = lambda: relu_hidden(SLABS + n)
                for j in range(pieces(t)):
                    beat(t, g, j, after[j], t == 2 and j == 2)

            slab(1, 0, ())
            slab(1, 1, ("sum", "norm"))
            with act.Fori(2, SLABS) as g:
                slab(1, g, ("sum", "norm"))

            slab(2, -1, ("sum", "norm"))
            slab(2, 0, ())
            with act.Fori(1, SLABS - 1) as g:
                slab(2, g, ("sum",))
            slab(2, SLABS - 1, ("sum",))
            copy_acc(2 * SLABS - 1)

        @block.vector
        def _(dve):
            NORM_STEPS = 10
            MIX_STEPS = 3
            DEGREE_STEPS = 4
            PASS2 = NORM_STEPS * SLABS + DEGREE_STEPS

            def link(base, j, ins):
                ins.then_inc(dve_step, 1)
                dve.wait_ge(dve_step, base + j)

            def norm_var(base, rows):
                for t in range(SUB):
                    last = dve.bn_stats(stats[:, t, :], rows[:, t, :])
                link(base, 1, last)
                link(base, 2, dve.tensor_tensor(gap[:, :], stats[:, :, 1], stats[:, :, 4], ALU.subtract))
                dve.tensor_tensor(squares[:, :], stats[:, :, 2], stats[:, :, 5], ALU.add)
                link(base, 3, dve.tensor_tensor(gap[:, :], gap[:, :], gap[:, :], ALU.mult))
                link(base, 4, dve.tensor_scalar(gap[:, :], gap[:, :], 0.25, EPS, ALU.mult, ALU.add))
                dve.scalar_tensor_tensor(var[:, :], squares[:, :], 1.0 / D, gap[:, :], ALU.mult, ALU.add)\
                   .then_inc(var_ready, 1)
                link(base, 5, dve.tensor_tensor(mean2[:, :], stats[:, :, 1], stats[:, :, 4], ALU.add))
                dve.scalar_tensor_tensor(centred[:, :, :], per_row(mean2[:, :]), -0.5, rows, ALU.mult, ALU.add)\
                   .then_inc(dve_step, 1)

            def norm_out(base, n):
                dve.wait_ge(rstd_seed, n + 1)
                link(base, 7, dve.tensor_tensor(rtmp[:, :], rstd[:, :], rstd[:, :], ALU.mult))
                link(base, 8, dve.tensor_tensor(rtmp[:, :], rtmp[:, :], var[:, :], ALU.mult))
                link(base, 9, dve.tensor_scalar(rtmp[:, :], rtmp[:, :], -0.5, 1.5, ALU.mult, ALU.add))
                link(base, 10, dve.tensor_tensor(rstd[:, :], rstd[:, :], rtmp[:, :], ALU.mult))
                wait(dve, hidden_turned, n)
                dve.tensor_tensor(hidden[:, :, :], centred[:, :, :], per_row(rstd[:, :]), ALU.mult)\
                   .then_inc(hidden_ready, 1)

            def row_sums(g, c):
                wait_loaded(dve, 0, g, c, 0)
                wait_loaded(dve, 0, g, c, 1)
                out = row_part[:, c, g] if isinstance(g, int) else row_part[:, c, bass.ds(g, 1)].squeeze(1)
                dve.reduce_sum(out, chunk[c][:, :].rearrange("p (s n) -> p s n", s=GROUPS), axis=AX.X).then_inc(summed, 1)

            def turn_chunk(t, g, c):
                n = CHUNKS * ((t - 1) * SLABS + g) + c
                for part in range(PARTS):
                    wait(dve, multiplied, KC * (n - 2) + KP * (part + 1) if not isinstance(n, int) or n >= 2 else 0)
                    ks = slice(part * KP, (part + 1) * KP)
                    dst = chunk_t[c % 2][:, ks, :].rearrange("p k (s r) -> p s k r", r=R)
                    if not (t == 2 and (c, 0) in MADE_IN[2]):
                        if part == 0:
                            wait_loaded(dve, t, g, c, 0)
                            wait_loaded(dve, t, g, c, 1)
                        last = dve.transpose(dst, chunk[c][:, :].rearrange("p (s k r) -> p s k r", r=R, k=KC)[:, :, ks])
                        last.then_inc(turned, 1)
                        continue
                    for h in range(2):
                        made_here = t == 2 and (c, h) in MADE_IN[2]
                        if made_here:
                            piece = (2, g, MADE_IN[2].index((c, h)))
                            src = odds[piece[2]]
                            if part == 0:
                                dve.wait_ge(weighed, number(piece) + 1)
                        else:
                            src = chunk[c][:, h * PIECE:(h + 1) * PIECE]
                            if part == 0:
                                wait_loaded(dve, t, g, c, h)
                        last = dve.transpose(dst[:, h * GROUPS // 2:(h + 1) * GROUPS // 2],
                                             src.rearrange("p (s k r) -> p s k r", r=R, k=KC)[:, :, ks])
                    last.then_inc(turned, 1)

            def mask(piece):
                t, g, r = piece
                c, h = MADE_IN[t][r]
                if t == 0:
                    slot_summed(dve, g, c)
                elif t == 1:
                    slot_turned(dve, 1, g, c)
                else:
                    wait_loaded(dve, 2, g, c, h)
                last = previous(piece)
                if last and last[0] < 2:
                    wait_spilled(dve, last)
                elif last:
                    slot_turned(dve, 2, last[1], MADE_IN[2][r][0])
                a = source(piece)
                dve.scalar_tensor_tensor(odds[r][:, :], a, 1.0, a, ALU.is_lt, ALU.mult).then_inc(masked, 1)

            def mix(n):
                base = PASS2 + (MIX_STEPS + NORM_STEPS) * n
                dve.wait_ge(acc_turned, n + 1)
                link(base, 1, dve.tensor_tensor(centred[:, :, :], xbank[:, :, :], of_slab(support, slab_of(1, n)), ALU.add))
                link(base, 2, dve.tensor_tensor(centred[:, :, :], centred[:, :, :], per_row(of_slab(dinv, slab_of(1, n))), ALU.mult))
                link(base, 3, dve.tensor_tensor(result[:, :, :], of_slab(tokens, slab_of(1, n)), centred[:, :, :], ALU.add))
                norm_var(base + MIX_STEPS, result[:, :, :])
                dve.tensor_copy(of_slab(tokens, slab_of(1, n)), result[:, :, :]).then_inc(x1_kept, 1)

            def give_message(n):
                dve.wait_ge(projected, SLABS + n + 1)
                dve.tensor_tensor(of_slab(message, slab_of(1, n)), xbank[:, :, :],
                                  bias[1][:, :].unsqueeze(1).to_broadcast([P, SUB, D]), ALU.add)\
                   .then_inc(message_ready, 1)

            def give_result(n):
                dve.wait_ge(acc_turned, SLABS + n + 1)
                wait(dve, stored, Q * 16 * n)
                dve.tensor_tensor(result[:, :, :], xbank[:, :, :], of_slab(tokens, n), ALU.add)\
                   .then_inc(result_ready, 1)

            def end_beat(turn, g, j):
                last = before(turn, g, j, 1)
                if last and (last[0], last[2]) not in POOL_DIVIDES:
                    divide(dve, last)

            def pass1(g):
                base = NORM_STEPS * g
                row_sums(g, 0)
                if isinstance(g, int):
                    dve.wait_ge(inputs_in, 8 * 16)
                norm_var(base, of_slab(tokens, g))
                row_sums(g, 3)
                mask((0, g, 0))
                row_sums(g, 1)
                mask((0, g, 1))
                row_sums(g, 2)
                norm_out(base, g)
                for j in range(pieces(0)):
                    if (0, j) not in POOL_DIVIDES:
                        divide(dve, (0, g, j))

            pass1(0)
            with dve.Fori(1, SLABS) as g:
                pass1(g)

            base = NORM_STEPS * SLABS
            dve.wait_ge(summed, CHUNKS * SLABS)
            dve.reduce_sum(row_sum, row_part.rearrange("p c g s -> p (g s) c"), axis=AX.X).then_inc(parts_added, 1)
            turn_chunk(1, 0, 0)
            dve.wait_ge(folded, 1)
            dve.tensor_scalar(degree[:, :], acc[:, 0:KB], 1.0, None, ALU.add).then_inc(degree_ready, 1)
            mask((1, 0, 0))
            dve.wait_ge(dinv_seed, 1)
            link(base, 1, dve.tensor_tensor(dtmp[:, :], dinv[:, :], dinv[:, :], ALU.mult))
            link(base, 2, dve.tensor_tensor(dtmp[:, :], dtmp[:, :], degree[:, :], ALU.mult))
            link(base, 3, dve.tensor_scalar(dtmp[:, :], dtmp[:, :], -0.5, 1.5, ALU.mult, ALU.add))
            link(base, 4, dve.tensor_tensor(dinv[:, :], dinv[:, :], dtmp[:, :], ALU.mult))
            dve.wait_ge(support_raw, SLABS)
            for n in range(KB // SUB):
                tiles = slice(n * SUB, (n + 1) * SUB)
                dve.tensor_tensor(support[:, tiles], support[:, tiles], per_row(dinv[:, tiles]), ALU.mult)\
                   .then_inc(support_ready, 1)
            turn_chunk(1, 0, 1)
            dve.wait_ge(support_ready, KB // SUB)
            end_beat(1, 0, 0)

            def slab1(g, from_beat=0):
                if from_beat == 0:
                    turn_chunk(1, g, 0)
                    mask((1, g, 0))
                    if not (isinstance(g, int) and g < 2):
                        give_message(g - 2)
                    turn_chunk(1, g, 1)
                    mix(g - 1)
                    end_beat(1, g, 0)
                mask((1, g, 1))
                turn_chunk(1, g, 2)
                if from_beat == 0:
                    norm_out(PASS2 + (MIX_STEPS + NORM_STEPS) * (g - 1) + MIX_STEPS, SLABS + g - 1)
                end_beat(1, g, 1)
                mask((1, g, 2))
                turn_chunk(1, g, 3)
                end_beat(1, g, 2)

            slab1(0, from_beat=1)
            dve.wait_ge(bias_added, 1)
            slab1(1)
            slab1(2)
            with dve.Fori(3, SLABS) as g:
                slab1(g)

            base = PASS2 + (MIX_STEPS + NORM_STEPS) * (SLABS - 1) + MIX_STEPS
            mask((2, 0, 0))
            give_message(SLABS - 2)
            mix(SLABS - 1)
            end_beat(2, -1, 0)
            norm_out(base, 2 * SLABS - 1)
            mask((2, 0, 1))
            end_beat(2, -1, 1)
            give_message(SLABS - 1)
            mask((2, 0, 2))
            turn_chunk(2, 0, 0)
            end_beat(2, -1, 2)

            def slab2(g):
                for j in range(pieces(2)):
                    if j > 0 or not (isinstance(g, int) and g == 0):
                        turn_chunk(2, g, j if j == 0 else j + 1)
                    if started(2, g, j):
                        mask(started(2, g, j))
                    if j == 0:
                        turn_chunk(2, g, 1)
                    if j == 1 and not (isinstance(g, int) and g == 0):
                        give_result(g - 1)
                    end_beat(2, g, j)

            slab2(0)
            dve.wait_ge(x1_kept, SLABS)
            with dve.Fori(1, SLABS - 1) as g:
                slab2(g)
            slab2(SLABS - 1)
            give_result(SLABS - 1)


_INS = ['x', 'adj', 'L0_gnn_weight', 'L0_gnn_bias', 'L1_gnn_W', 'L1_gnn_B']
_OUTS = [((N, D), 'float32')]


def kernel(**inputs):
    import numpy as _np
    import concourse.bacc as _bacc
    from concourse import mybir as _mybir
    from concourse.bass_utils import run_bass_kernel_spmd as _run

    nc = _bacc.Bacc("TRN2", target_bir_lowering=False, num_devices=1)
    arrays, args = {}, []
    for name in _INS:
        a = _np.ascontiguousarray(inputs[name])
        arrays[f"in_{name}_dram"] = a
        args.append(nc.dram_tensor(f"in_{name}_dram", a.shape, _mybir.dt.from_np(a.dtype), kind="ExternalInput").ap())
    for i, (shape, dtype) in enumerate(_OUTS):
        dt = _mybir.dt.from_np(_np.dtype(dtype))
        args.append(nc.dram_tensor(f"out_{i}_dram", shape, dt, kind="ExternalOutput").ap())
    graph_layers(nc, *args)
    r = _run(nc, [arrays], core_ids=[0])
    return r.results[0]["out_0_dram"]
```
